# Optimizing a Trainium2 kernel written in Bass

```python
import numpy as np
import jax
import jax.numpy as jnp

def _softmax(x, axis=-1):
    return jax.nn.softmax(x, axis=axis)

def _gelu(x):
    return jax.nn.gelu(x, approximate=True)

def _silu(x):
    return jax.nn.silu(x)

def _sigmoid(x):
    return jax.nn.sigmoid(x)

def _layernorm(x, axis=-1, eps=1e-05):
    m = jnp.mean(x, axis=axis, keepdims=True)
    v = jnp.var(x, axis=axis, keepdims=True)
    return (x - m) / jnp.sqrt(v + eps)

def _scatter_add(tgt, idx, src, axis=0):
    return tgt.at[idx].add(src)

def _segment_sum(src, seg, n):
    return jax.ops.segment_sum(src, seg, n)
kernel_name = 'mk_gnn_ffn_d1_gnn_r8_dc831d'

def setup_inputs(seed: int=0):
    np.random.seed(seed)
    _w = jnp.asarray

    def _rec_inputs():
        import jax
        import jax.numpy as jnp
        _gk = jax.random.key(seed)
        x = -0.0002117 + 1 * jax.random.normal(jax.random.fold_in(_gk, 1), (12500, 256), jnp.float32)
        src = jax.random.randint(jax.random.fold_in(_gk, 2), (200000,), 0, 12500, jnp.int32)
        dst = jax.random.randint(jax.random.fold_in(_gk, 3), (200000,), 0, 12500, jnp.int32)
        _o = jnp.argsort(dst, stable=True)
        src = src[_o]
        dst = dst[_o]
        edge_weight = jax.random.uniform(jax.random.fold_in(_gk, 12), (200000,), jnp.float32, 0.0, 0.999998)
        return (x, src, dst, edge_weight)
    x, src, dst, edge_weight = _rec_inputs()

    def _L0_gnn_setup():
        import jax, jax.numpy as jnp
        import numpy as np
        N_NODES = 12500
        N_EDGES = 37500
        D = 256
        EPS = 1e-05
        ALPHA = 0.5

        def gcn_residual(x, edge_index, edge_weight, W, b, gamma, beta):
            src, dst = (edge_index[0], edge_index[1])
            h = x @ W
            deg = jax.ops.segment_sum(edge_weight, dst, num_segments=N_NODES) + 1.0
            dinv = jax.lax.rsqrt(deg)
            norm = dinv[src] * edge_weight * dinv[dst]
            agg = jax.ops.segment_sum(norm[:, None] * h[src], dst, num_segments=N_NODES)
            agg = agg + (dinv * dinv)[:, None] * h
            h = agg + b
            mu = jnp.mean(h, axis=-1, keepdims=True)
            var = jnp.mean(jnp.square(h - mu), axis=-1, keepdims=True)
            h = (h - mu) * jax.lax.rsqrt(var + EPS) * gamma + beta
            h = ALPHA * h + (1.0 - ALPHA) * x
            return jax.nn.relu(h)
        key = jax.random.key(seed)
        ks = jax.random.split(key, 6)
        x = jax.random.normal(ks[0], (N_NODES, D), dtype=jnp.float32)
        edge_index = jax.random.randint(ks[1], (2, N_EDGES), 0, N_NODES, dtype=jnp.int32)
        edge_weight = jax.random.uniform(ks[2], (N_EDGES,), dtype=jnp.float32)
        W = jax.random.normal(ks[3], (D, D), dtype=jnp.float32) / np.float32(np.sqrt(D))
        b = 0.01 * jax.random.normal(ks[4], (D,), dtype=jnp.float32)
        gamma = jnp.ones((D,), dtype=jnp.float32)
        beta = jnp.zeros((D,), dtype=jnp.float32)
        return {'x': x, 'edge_index': edge_index, 'edge_weight': edge_weight, 'W': W, 'b': b, 'gamma': gamma, 'beta': beta}
    _L0_gnn_all = _L0_gnn_setup()
    _L0_gnn_in = {k: v for k, v in _L0_gnn_all.items() if k in ('W', 'b', 'gamma', 'beta')}
    del _L0_gnn_all

    def _L0_ffn_setup():
        import jax, jax.numpy as jnp
        import numpy as np
        E = 8
        K = 2
        D = 256
        H = 512
        DOUT = 256
        EPS = 1e-05
        key = jax.random.key(seed)
        ks = jax.random.split(key, 9)
        s = 0.02
        return {'x': jax.random.normal(ks[0], (4, 1024, D), jnp.float32), 'gamma': 1.0 + 0.05 * jax.random.normal(ks[1], (D,), jnp.float32), 'beta': 0.05 * jax.random.normal(ks[2], (D,), jnp.float32), 'Wr': 0.01 * jax.random.normal(ks[3], (D, E), jnp.float32), 'br': jnp.zeros((E,), jnp.float32), 'W1': s * jax.random.normal(ks[4], (E, D, H), jnp.float32), 'b1': s * jax.random.normal(ks[5], (E, H), jnp.float32), 'W2': s * jax.random.normal(ks[6], (E, H, DOUT), jnp.float32), 'b2': s * jax.random.normal(ks[7], (E, DOUT), jnp.float32)}
    _L0_ffn_all = _L0_ffn_setup()
    _L0_ffn_in = {k: v for k, v in _L0_ffn_all.items() if k in ('gamma', 'beta', 'Wr', 'br', 'W1', 'b1', 'W2', 'b2')}
    del _L0_ffn_all
    return {'x': x, 'src': src, 'dst': dst, 'edge_weight': edge_weight, 'L0_gnn_W': _L0_gnn_in['W'], 'L0_gnn_b': _L0_gnn_in['b'], 'L0_gnn_gamma': _L0_gnn_in['gamma'], 'L0_gnn_beta': _L0_gnn_in['beta'], 'L0_ffn_gamma': _L0_ffn_in['gamma'], 'L0_ffn_beta': _L0_ffn_in['beta'], 'L0_ffn_Wr': _L0_ffn_in['Wr'], 'L0_ffn_br': _L0_ffn_in['br'], 'L0_ffn_W1': _L0_ffn_in['W1'], 'L0_ffn_b1': _L0_ffn_in['b1'], 'L0_ffn_W2': _L0_ffn_in['W2'], 'L0_ffn_b2': _L0_ffn_in['b2']}

def reference(x, src, dst, edge_weight, L0_gnn_W, L0_gnn_b, L0_gnn_gamma, L0_gnn_beta, L0_ffn_gamma, L0_ffn_beta, L0_ffn_Wr, L0_ffn_br, L0_ffn_W1, L0_ffn_b1, L0_ffn_W2, L0_ffn_b2):
    import jax
    import jax.numpy as jnp

    def _L0_gnn_ref(x, edge_index, edge_weight, W, b, gamma, beta):
        import jax, jax.numpy as jnp
        import numpy as np
        N_NODES = 12500
        N_EDGES = 37500
        D = 256
        EPS = 1e-05
        ALPHA = 0.5

        def gcn_residual(x, edge_index, edge_weight, W, b, gamma, beta):
            src, dst = (edge_index[0], edge_index[1])
            h = x @ W
            deg = jax.ops.segment_sum(edge_weight, dst, num_segments=N_NODES) + 1.0
            dinv = jax.lax.rsqrt(deg)
            norm = dinv[src] * edge_weight * dinv[dst]
            agg = jax.ops.segment_sum(norm[:, None] * h[src], dst, num_segments=N_NODES)
            agg = agg + (dinv * dinv)[:, None] * h
            h = agg + b
            mu = jnp.mean(h, axis=-1, keepdims=True)
            var = jnp.mean(jnp.square(h - mu), axis=-1, keepdims=True)
            h = (h - mu) * jax.lax.rsqrt(var + EPS) * gamma + beta
            h = ALPHA * h + (1.0 - ALPHA) * x
            return jax.nn.relu(h)
        return gcn_residual(x, edge_index, edge_weight, W, b, gamma, beta)

    def _L0_ffn_ref(x, gamma, beta, Wr, br, W1, b1, W2, b2):
        import jax, jax.numpy as jnp
        import numpy as np
        E = 8
        K = 2
        D = 256
        H = 512
        DOUT = 256
        EPS = 1e-05
        mu = jnp.mean(x, axis=-1, keepdims=True)
        var = jnp.mean(jnp.square(x - mu), axis=-1, keepdims=True)
        xn = (x - mu) * jax.lax.rsqrt(var + EPS) * gamma + beta
        logits = jnp.einsum('bsd,de->bse', xn, Wr) + br
        top_vals, top_idx = jax.lax.top_k(logits, K)
        w = jax.nn.softmax(top_vals, axis=-1)
        w_full = jnp.einsum('bsk,bske->bse', w, jax.nn.one_hot(top_idx, E, dtype=w.dtype))
        y = jnp.zeros(x.shape[:-1] + (DOUT,), x.dtype)
        for e in range(E):
            h = jax.nn.gelu(jnp.einsum('bsd,dh->bsh', xn, W1[e]) + b1[e], approximate=False)
            y_e = jnp.einsum('bsh,hd->bsd', h, W2[e]) + b2[e]
            y = y + y_e * w_full[..., e, None]
        return y
    edge_index = jnp.stack([src, dst])
    x = x + _L0_gnn_ref(_layernorm(x, axis=-1), edge_index, edge_weight, L0_gnn_W, L0_gnn_b, L0_gnn_gamma, L0_gnn_beta)
    x = x + _L0_ffn_ref(_layernorm(x, axis=-1)[None], L0_ffn_gamma, L0_ffn_beta, L0_ffn_Wr, L0_ffn_br, L0_ffn_W1, L0_ffn_b1, L0_ffn_W2, L0_ffn_b2)[0]
    return x

_drawn_inputs = setup_inputs


def setup_inputs(seed=0):
    import zlib

    import numpy as np

    out = dict(_drawn_inputs(seed))
    spreads = {'L0_gnn_gamma': (1.0, 0.2), 'L0_gnn_beta': (0.0, 0.297), 'L0_ffn_br': (0.0, 0.1)}
    factors = {'L0_gnn_b': 6.013,
     'L0_ffn_gamma': 8.0,
     'L0_ffn_beta': 6.616,
     'L0_ffn_b1': 8.0,
     'L0_ffn_b2': 5.599}
    for name, (base, spread) in spreads.items():
        noise = np.random.default_rng([zlib.crc32(name.encode()), seed]).standard_normal(out[name].shape)
        drawn = base * np.exp(spread * noise) if base else spread * noise
        out[name] = jnp.asarray(drawn.astype(out[name].dtype))
    for name, factor in factors.items():
        out[name] = (out[name] * factor).astype(out[name].dtype)
    return out
```

```python
from contextlib import ExitStack

import concourse.bass as bass
from concourse import mybir

F32 = mybir.dt.float32
F32R = mybir.dt.float32r
BF16 = mybir.dt.bfloat16
I32 = mybir.dt.int32
U32 = mybir.dt.uint32
ALU = mybir.AluOpType
ACT = mybir.ActivationFunctionType
AX = mybir.AxisListType

N_NODES, D = 12500, 256
N_EDGES = 200000
N_EXPERTS, HIDDEN = 8, 512
EPS = 1e-5

P = 128
BLK = 125
GT = 4
GRP = BLK * GT
BLOCKS = N_NODES // BLK
GROUPS = N_NODES // GRP
KD = D // P
KH = HIDDEN // P
STEPS = N_EXPERTS * KH
QS = STEPS // GT
CARRY = 12

UNIT = 32
UNITS = N_EDGES // UNIT
EP = 125
EC = N_EDGES // EP
UC = EC // UNIT
TILES = 17
TILE_UNITS = P // UNIT
MAX_EXTRA = -(-(UNITS - TILES * TILE_UNITS) // TILE_UNITS)
PAD = 2304
EDGES_P = N_EDGES + PAD
SLOTS = 4

DVE_STAGES = ("conv", "conv_stats", "conv_mv", "conv_rs", "conv_nm", "x_biased", "scaled", "mixed",
              "x1", "x1_stats", "x1_mv", "x1_rs", "x1_nm", "xl_stats", "xl_mv", "xl_rs", "xl_nm",
              "xf0", "xlow0", "xf1", "xlow1", "logits_low", "logits", "top", "top_i", "top_f", "gap", "denom",
              "w_first", "w_second", "gate_first", "gate_second", "gates", "y01", "y23")
ACT_STAGES = ("x_half", "conv_sd", "conv_n", "x1_sd", "xl", "xl_sd", "xl2", "xhigh0", "xhigh1",
              "exp", "gates_t")
PE_STAGES = ("xt0", "xt1", "logits", "gates_t", "b2_01", "b2_23")


def extra_tile(nc, first, k):
    return nc.s_assert_within(first + k * P + P * TILES, 0, EDGES_P - P,
                              skip_runtime_bounds_check_because="extra tiles end less than a tile past the range")


class Stages:

    def __init__(self, sem, names, credit=0):
        self.sem, self.names, self.credit = sem, names, credit

    def after(self, group, name):
        n = len(self.names)
        return (group + self.credit) * n + (self.names.index(name) + 1)




def wait(eng, sem, value):
    if not isinstance(value, int) or value > 0:
        eng.wait_ge(sem, value)


def build(nc, x, src, dst, edge_weight, w_gnn, b_gnn, gamma_gnn, beta_gnn, gamma_ffn, beta_ffn,
          w_route, b_route, w1, b1, w2, b2, out):
    stack = ExitStack()
    with stack:
        def dram(name, shape, dt):
            return nc.dram_tensor(name, shape, dt).ap()

        def sem(name):
            return stack.enter_context(nc.semaphore(name))

        def sbuf(name, shape, dt, into=stack):
            return into.enter_context(nc.sbuf_tensor(name, shape, dt))

        def psum(name, shape, dt, into=stack):
            return into.enter_context(nc.psum_tensor(name, shape, dt))

        src_p = dram("src_padded", [EDGES_P], I32)
        dst_p = dram("dst_padded", [EDGES_P], I32)
        w_p = dram("weight_padded", [EDGES_P], F32)
        w3_p = dram("weight_parts", [EDGES_P * 3], BF16)
        unit_minmax = dram("unit_minmax", [2, UNITS], F32)
        ranges_d = dram("ranges", [BLOCKS, 4], I32)
        table = dram("node_table", [N_NODES, D], F32)

        ranges = sbuf("ranges_sb", [1, BLOCKS * 4], I32)
        block_base = sbuf("block_base", [P, BLOCKS], F32)
        dinv = sbuf("dinv", [BLK, BLOCKS], F32)
        x_rs_half = sbuf("x_rs_half", [BLK, BLOCKS], F32)
        x_nm_half = sbuf("x_nm_half", [BLK, BLOCKS], F32)
        ident = sbuf("ident", [P, P], F32)
        eps = sbuf("eps", [P, 1], F32)

        def load_rows(eng, to, of, done):
            eng.dma_start(to[0:112], of[0:112]).then_inc(done, 16)
            eng.dma_start(to[112:BLK], of[112:BLK]).then_inc(done, 16)

        phase_1(nc, sbuf, psum, sem, src, dst, edge_weight, src_p, dst_p, w_p, w3_p,
                unit_minmax, ranges_d, ranges, block_base, ident, eps, load_rows)
        wts = experts_on_chip(sbuf)
        phase_2(nc, sbuf, psum, sem, x, w_gnn, w1, w2, w_route, dst_p, w3_p, table, ranges,
                block_base, dinv, x_rs_half, x_nm_half, ident, eps, wts, load_rows)
        phase_3(nc, sbuf, psum, sem, x, src_p, dst_p, w_p, table, b_gnn, gamma_gnn, beta_gnn,
                gamma_ffn, beta_ffn, b_route, b1, b2, out, ranges, block_base, dinv, x_rs_half,
                x_nm_half, ident, eps, wts, load_rows)


def phase_1(nc, sbuf, psum, sem, src, dst, edge_weight, src_p, dst_p, w_p, w3_p, unit_minmax,
            ranges_d, ranges, block_base, ident, eps, load_rows):
    with ExitStack() as mem:
        dst_sb = sbuf("dst_all", [EP, EC], I32, mem)
        w_sb = sbuf("weight_all", [EP, EC], F32, mem)
        rest1 = sbuf("weight_rest1", [EP, EC], F32, mem)
        rest2 = sbuf("weight_rest2", [EP, EC], F32, mem)
        w3 = sbuf("weight_parts_sb", [EP, EC, 3], BF16, mem)
        minus = sbuf("minus_ones", [16, PAD // 16], I32, mem)
        zeros = sbuf("zeros", [16, PAD // 16], F32, mem)
        zeros3 = sbuf("zeros3", [16, PAD * 3 // 16], BF16, mem)
        mm = sbuf("minmax", [EP, 2, UC], F32, mem)
        rows = sbuf("minmax_rows", [BLOCKS, 2, UNITS], F32, mem)
        place = sbuf("unit_place", [BLOCKS, UNITS], F32, mem)
        first_i = sbuf("first_node_i", [BLOCKS, 1], I32, mem)
        first = sbuf("first_node", [BLOCKS, 1], F32, mem)
        last = sbuf("last_node", [BLOCKS, 1], F32, mem)
        base_i = sbuf("block_base_i", [P, BLOCKS], I32, mem)
        hi = sbuf("range_hi", [BLOCKS, 1], F32, mem)
        lo_m = sbuf("range_lo_mirrored", [BLOCKS, 1], F32, mem)
        span = sbuf("range_span", [BLOCKS, 1], F32, mem)
        extra = sbuf("range_extra", [BLOCKS, 1], F32, mem)
        entry = sbuf("range_entry", [BLOCKS, 4], I32, mem)
        before = sbuf("strictly_before", [BLOCKS, BLOCKS], F32, mem)
        prefix = psum("extra_prefix", [BLOCKS, 1], F32, mem)

        dst_in, w_in, copied, consts = sem("dst_in"), sem("w_in"), sem("copied"), sem("consts1")
        minmax_ready, minmax_out = sem("minmax_ready"), sem("minmax_out")
        rows_in, w3_ready = sem("rows_in"), sem("w3_ready")
        chain, extra_ready, prefix_ready = sem("dve_chain1"), sem("extra_ready"), sem("prefix_ready")
        entry_ready, entry_out, ranges_in = sem("entry_ready"), sem("entry_out"), sem("ranges_in")
        ident_zero, before_one = sem("ident_zero"), sem("before_one")

        with nc.Block() as block:
            @block.sync
            def _(sp):
                load_rows(sp, dst_sb, dst.rearrange("(p c) -> p c", p=EP), dst_in)
                load_rows(sp, w_sb, edge_weight.rearrange("(p c) -> p c", p=EP), w_in)
                sp.wait_ge(minmax_ready, 2)
                load_rows(sp, unit_minmax.rearrange("c (p k) -> p c k", p=EP), mm, minmax_out)
                sp.wait_ge(minmax_out, 32)
                sp.dma_start(rows[:, :, :].rearrange("p c s -> p (c s)"),
                             unit_minmax.rearrange("c s -> (c s)").partition_broadcast(BLOCKS))\
                  .then_inc(rows_in, 16)
                sp.wait_ge(w3_ready, 1)
                load_rows(sp, w3_p[0:N_EDGES * 3].rearrange("(p c) -> p c", p=EP),
                          w3[:, :, :].rearrange("p c k -> p (c k)"), copied)
                sp.wait_ge(entry_ready, 1)
                sp.dma_start(ranges_d, entry[:, :]).then_inc(entry_out, 16)
                sp.wait_ge(entry_out, 16)
                sp.dma_start(ranges[:, :], ranges_d.rearrange("(o b) c -> o (b c)", o=1))\
                  .then_inc(ranges_in, 16)
                sp.wait_ge(ranges_in, 16)
                sp.wait_ge(copied, 32 + 16 * 7)

            @block.gpsimd
            def _(pool):
                pool.iota(place[:, :], [[1, UNITS]], base=1, channel_multiplier=0,
                          allow_small_or_imprecise_dtypes=True).then_inc(consts, 1)
                pool.iota(first_i[:, :], [[0, 1]], base=0, channel_multiplier=BLK).then_inc(consts, 1)
                pool.iota(base_i[:, :], [[BLK, BLOCKS]], base=0, channel_multiplier=0).then_inc(consts, 1)
                pool.memset(before[:, :], 1.0).then_inc(before_one, 1)
                pool.memset(ident[:, :], 0.0).then_inc(ident_zero, 1)
                pool.memset(eps[:, :], EPS).then_inc(consts, 1)
                pool.wait_ge(before_one, 1)
                pool.affine_select(out=before[:, :], in_=before[:, :], compare_op=ALU.is_gt, fill=0.0,
                                   base=0, pattern=[[1, BLOCKS]], channel_multiplier=-1)\
                    .then_inc(consts, 1)
                pool.wait_ge(ident_zero, 1)
                pool.affine_select(out=ident[:, :], in_=ident[:, :], compare_op=ALU.not_equal, fill=1.0,
                                   base=0, pattern=[[-1, P]], channel_multiplier=1)\
                    .then_inc(consts, 1)

            @block.scalar
            def _(act):
                for to, of in ((src_p, src), (dst_p, dst), (w_p, edge_weight)):
                    act.dma_start(to[0:N_EDGES].rearrange("(a b) -> a b", a=80),
                                  of.rearrange("(a b) -> a b", a=80)).then_inc(copied, 16)
                act.wait_ge(consts, 9)
                for to, of in ((src_p, zeros[:, :].bitcast(I32)), (dst_p, minus[:, :]), (w_p, zeros[:, :])):
                    act.dma_start(to[N_EDGES:EDGES_P].rearrange("(a b) -> a b", a=16), of)\
                       .then_inc(copied, 16)
                act.dma_start(w3_p[N_EDGES * 3:EDGES_P * 3].rearrange("(a b) -> a b", a=16),
                              zeros3[:, :]).then_inc(copied, 16)

            @block.tensor
            def _(pe):
                pe.wait_ge(consts, 9)
                pe.wait_ge(extra_ready, 1)
                nc.tensor.matmul(prefix[:, :], before[:, :], extra[:, :], start=True, stop=True)\
                  .then_inc(prefix_ready, 1)

            @block.vector
            def _(dve):
                steps = [0]

                def link(ins):
                    steps[0] += 1
                    ins.then_inc(chain, 1)
                    dve.wait_ge(chain, steps[0])

                dve.memset(minus[:, :], -1).then_inc(consts, 1)
                dve.memset(zeros[:, :], 0.0).then_inc(consts, 1)
                dve.memset(zeros3[:, :], 0.0).then_inc(consts, 1)
                dve.wait_ge(dst_in, 32)
                for c, op in ((0, ALU.max), (1, ALU.min)):
                    dve.tensor_reduce(mm[:, c, :], dst_sb[:, :].rearrange("p (k u) -> p k u", u=UNIT),
                                      AX.X, op).then_inc(minmax_ready, 1)
                dve.wait_ge(w_in, 32)
                link(dve.tensor_copy(w3[:, :, 0], w_sb[:, :]))
                link(dve.tensor_tensor(rest1[:, :], w_sb[:, :], w3[:, :, 0], ALU.subtract))
                link(dve.tensor_copy(w3[:, :, 1], rest1[:, :]))
                link(dve.tensor_tensor(rest2[:, :], rest1[:, :], w3[:, :, 1], ALU.subtract))
                dve.tensor_copy(w3[:, :, 2], rest2[:, :]).then_inc(w3_ready, 1)
                dve.wait_ge(consts, 9)
                dve.tensor_copy(block_base[:, :], base_i[:, :])
                link(dve.tensor_copy(first[:, :], first_i[:, :]))
                link(dve.tensor_scalar(last[:, :], first[:, :], float(BLK - 1), None, ALU.add))
                dve.wait_ge(rows_in, 16)
                link(dve.scalar_tensor_tensor(rows[:, 1, :], rows[:, 1, :], last[:, 0:1], place[:, :],
                                              ALU.is_le, ALU.mult))
                dve.tensor_reduce(hi[:, :], rows[:, 1, :], AX.X, ALU.max)
                link(dve.tensor_scalar(place[:, :], place[:, :], -1.0, float(UNITS + 1), ALU.mult, ALU.add))
                link(dve.scalar_tensor_tensor(rows[:, 0, :], rows[:, 0, :], first[:, 0:1], place[:, :],
                                              ALU.is_ge, ALU.mult))
                link(dve.tensor_reduce(lo_m[:, :], rows[:, 0, :], AX.X, ALU.max))
                link(dve.tensor_scalar(entry[:, 0:1], lo_m[:, :], -float(UNIT), float(UNITS * UNIT),
                                       ALU.mult, ALU.add))
                link(dve.tensor_tensor(span[:, :], hi[:, :], lo_m[:, :], ALU.add))
                shift = -float(UNITS + TILES * TILE_UNITS - (TILE_UNITS - 1))
                link(dve.tensor_scalar(span[:, :], span[:, :], shift, 1.0 / TILE_UNITS, ALU.add, ALU.mult))
                link(dve.tensor_scalar(span[:, :], span[:, :], -0.375, 0.0, ALU.add, ALU.max))
                link(dve.tensor_copy(entry[:, 1:2], span[:, :]))
                dve.memset(entry[:, 3:4], 0)
                link(dve.tensor_copy(extra[:, :], entry[:, 1:2]))
                dve.sem_inc(extra_ready, 1)
                dve.wait_ge(prefix_ready, 1)
                dve.tensor_copy(entry[:, 2:3], prefix[:, :]).then_inc(entry_ready, 1)


def experts_on_chip(sbuf):
    return {name: sbuf(name, shape, F32R) for name, shape in (
        ("w1_high", [P, N_EXPERTS, KD, HIDDEN]), ("w1_low", [P, N_EXPERTS, KD, HIDDEN]),
        ("w2_high", [P, N_EXPERTS, KH, D]), ("w2_low", [P, N_EXPERTS, KH, D]),
        ("wr", [P, KD, 2, N_EXPERTS]))}


def first_edge(eng, ranges, blk):
    return eng.value_load(ranges[0:1, bass.ds(blk * 4, 1)], min_val=0, max_val=N_EDGES)


def extra_tiles(eng, ranges, blk):
    return eng.value_load(ranges[0:1, bass.ds(blk * 4 + 1, 1)], min_val=0, max_val=MAX_EXTRA)


def extra_before(eng, ranges, blk):
    return eng.value_load(ranges[0:1, bass.ds(blk * 4 + 2, 1)], min_val=0, max_val=MAX_EXTRA * BLOCKS)


def phase_2(nc, sbuf, psum, sem, x, w_gnn, w1, w2, w_route, dst_p, w3_p, table, ranges, block_base,
            dinv, x_rs_half, x_nm_half, ident, eps, wts, load_rows):
    TP = TILES + 1
    RING = 4
    UNROLL = 5
    with ExitStack() as mem:
        place_i = sbuf("node_place_i", [P, BLK], I32, mem)
        node_place = sbuf("node_place", [P, BLK, TP], BF16, mem)
        dst_t = sbuf("dst_tiles", [P, RING, TILES], I32, mem)
        w3_t = sbuf("weight_tiles", [P, RING, TILES, 3], BF16, mem)
        local = sbuf("dst_local", [P, RING, TP], BF16, mem)
        member = sbuf("member", [P, RING, BLK, TP], BF16, mem)
        dst_e = sbuf("dst_extra", [P, 1], I32, mem)
        w3_e = sbuf("weight_extra", [P, 3], BF16, mem)
        local_e = sbuf("dst_local_extra", [P, 1], F32, mem)
        member_e = sbuf("member_extra", [P, BLK], BF16, mem)
        deg = sbuf("degree", [BLK, BLOCKS], F32, mem)
        deg_ps = psum("degree_parts", [BLK, BLOCKS, 3], F32, mem)
        raw = sbuf("raw_weights", [P, 1, KD * HIDDEN], F32, mem)
        raw_r = sbuf("raw_route", [P, KD, N_EXPERTS], F32, mem)
        wg = sbuf("w_gnn_sb", [P, KD, D], F32, mem)
        x_sb = sbuf("x_in", [BLK, UNROLL, GT, D], F32, mem)
        xn = sbuf("xn", [BLK, 2, GT, D], F32, mem)
        xt = sbuf("xt", [P, KD, GRP], F32, mem)
        t_sb = sbuf("t_out", [BLK, GT, D], F32, mem)
        st = sbuf("x_stats", [BLK, GT, 6], F32, mem)
        mv = sbuf("x_mean_var", [BLK, GT, 2], F32, mem)
        sd = sbuf("x_sd", [BLK, GT], F32, mem)
        rs = sbuf("x_rs", [BLK, GT], F32, mem)
        nm = sbuf("x_nm", [BLK, GT], F32, mem)
        xt_ps = [psum(f"xt_ps{k}", [P, 512], F32, mem) for k in range(KD)]
        h_ps = [psum(f"h_ps{k}", [BLK, 2, D], F32, mem) for k in range(2)]

        tiles_in = [sem(f"tiles_in{q}") for q in range(RING)]
        place_ready, place_cast, settled = sem("place_ready"), sem("place_cast"), sem("settled2")
        local_ready, member_ready = sem("local_ready"), sem("member_ready")
        block_summed = sem("block_summed")
        extra_in, extra_local, extra_member = sem("extra_in2"), sem("extra_local2"), sem("extra_member2")
        extra_summed = sem("extra_summed")
        deg_done, dinv_done = sem("deg_done"), sem("dinv_done")
        raw_in, high_done, low_done, route_in = sem("raw_in"), sem("high_done"), sem("low_done"), sem("route_in")
        x_in = [sem(f"x_in_{u}") for u in range(UNROLL)]
        t_stored = sem("t_stored")
        dve_ahead = Stages(sem("dve_ahead"), ("stats", "mean_var", "rs", "nm", "rs_half", "nm_half"), 1)
        on_dve = Stages(sem("dve_stage2"), ("xt1", "t"), 1)
        act_ahead = Stages(sem("act_ahead"), ("sd", "xn"), UNROLL)
        on_act = Stages(sem("act_stage2"), ("xt0",), 1)
        on_xt = Stages(sem("pe_transposed"), ("xt",), 2)
        on_h = Stages(sem("pe_product"), ("h",), 1)

        def raw_parts(e):
            if e % 2 == 0:
                return (w1[e // 2].rearrange("(c p) h -> p c h", p=P), KD,
                        wts["w1_high"][:, e // 2], wts["w1_low"][:, e // 2])
            return (w2[e // 2].rearrange("(c p) h -> p c h", p=P), KH,
                    wts["w2_high"][:, e // 2], wts["w2_low"][:, e // 2])

        def raw_view(c):
            return raw[:, 0, :].rearrange("p (c h) -> p c h", c=c)

        with nc.Block() as block:
            @block.sync
            def _(sp):
                with nc.sync.Fori(0, BLOCKS // RING) as i:
                    for q in range(RING):
                        blk = i * RING + q
                        first = first_edge(sp, ranges, blk)
                        extra = extra_tiles(sp, ranges, blk)
                        at, at3 = sp.snap(first), sp.snap(first * 3)
                        sp.wait_ge(block_summed, blk + 1)
                        sp.sem_inc(settled, 1)
                        sp.dma_start(dst_t[:, q, :], dst_p[bass.ds(at, P * TILES)]
                                     .rearrange("(p j) -> p j", j=TILES)).then_inc(tiles_in[q], 16)
                        sp.dma_start(w3_t[:, q, :, :].rearrange("p j k -> p (j k)"),
                                     w3_p[bass.ds(at3, P * TILES * 3)]
                                     .rearrange("(p j) -> p j", j=TILES * 3)).then_inc(tiles_in[q], 16)
                        with nc.sync.If(extra > 0):
                            done = extra_before(sp, ranges, blk)
                            with nc.sync.Fori(0, extra) as k:
                                a = sp.snap(extra_tile(nc, first, k))
                                a3 = sp.snap(a * 3)
                                sp.wait_ge(extra_summed, done + k + 1)
                                sp.sem_inc(settled, 1)
                                sp.dma_start(dst_e[:, :], dst_p[bass.ds(a, P)]
                                             .rearrange("(p j) -> p j", j=1)).then_inc(extra_in, 16)
                                sp.dma_start(w3_e[:, :], w3_p[bass.ds(a3, P * 3)]
                                             .rearrange("(p j) -> p j", j=3)).then_inc(extra_in, 16)
                            sp.sem_inc(settled, 1)
                with nc.sync.Fori(0, GROUPS // UNROLL) as i:
                    for u in range(UNROLL):
                        sp.wait_ge(act_ahead.sem, act_ahead.after(i * UNROLL + u - UNROLL, "xn"))
                        sp.sem_inc(settled, 1)
                        load_rows(sp, x_sb[:, u], x[bass.ds(i * (UNROLL * GRP) + u * GRP, GRP), :]
                                  .rearrange("(t p) d -> p t d", p=BLK), x_in[u])

            @block.scalar
            def _(act):
                act.sem_inc(act_ahead.sem, UNROLL * len(act_ahead.names))
                act.sem_inc(on_act.sem, 1)
                act.sem_inc(t_stored, 32)
                act.dma_start(wg[:, :, :], w_gnn.rearrange("(c p) n -> p c n", p=P)).then_inc(route_in, 16)
                act.dma_start(raw_r[:, :, :], w_route.rearrange("(c p) n -> p c n", p=P)).then_inc(route_in, 16)
                act.wait_ge(route_in, 32)
                act.activation(wts["wr"][:, :, 0, :], raw_r[:, :, :], ACT.Copy).then_inc(high_done, 1)
                for e in range(2 * N_EXPERTS):
                    of, c, high, _low = raw_parts(e)
                    act.wait_ge(low_done, e + 1)
                    act.dma_start(raw_view(c), of).then_inc(raw_in, 16)
                    act.wait_ge(raw_in, 16 * (e + 1))
                    act.activation(high, raw_view(c), ACT.Copy).then_inc(high_done, 1)
                act.wait_ge(deg_done, 4)
                act.activation(deg[:, :], deg[:, :], ACT.Sqrt).then_inc(dinv_done, 1)

                def normalise(i, u):
                    g = i * UNROLL + u
                    act.wait_ge(dve_ahead.sem, dve_ahead.after(g, "mean_var"))
                    act.activation(sd[:, :], mv[:, :, 1], ACT.Sqrt, bias=eps[0:BLK, :]).then_inc(act_ahead.sem, 1)
                    act.wait_ge(dve_ahead.sem, dve_ahead.after(g, "nm"))
                    act.wait_ge(on_xt.sem, on_xt.after(g - (2 if u else 1), "xt"))
                    for t in range(GT):
                        ins = act.activation(xn[:, u % 2, t, :], x_sb[:, u, t, :], ACT.Identity,
                                             bias=nm[:, t:t + 1], scale=rs[:, t:t + 1])
                    ins.then_inc(act_ahead.sem, 1)

                with nc.scalar.Fori(0, GROUPS // UNROLL) as i:
                    normalise(i, 0)
                    for u in range(UNROLL):
                        g = i * UNROLL + u
                        if u + 1 < UNROLL:
                            normalise(i, u + 1)
                        act.wait_ge(on_xt.sem, on_xt.after(g, "xt"))
                        act.wait_ge(on_h.sem, on_h.after(g - 1, "h"))
                        act.activation(xt[:, 0, :], xt_ps[0][:, 0:GRP], ACT.Copy).then_inc(on_act.sem, 1)
                        at = act.snap(g * GRP)
                        act.wait_ge(on_dve.sem, on_dve.after(g, "t"))
                        load_rows(act, table[bass.ds(at, GRP), :].rearrange("(t p) d -> p t d", p=BLK),
                                  t_sb, t_stored)
                act.wait_ge(t_stored, 32 * (GROUPS + 1))

            @block.gpsimd
            def _(pool):
                pool.iota(place_i[:, :], [[1, BLK]], base=0, channel_multiplier=0).then_inc(place_ready, 1)
                pool.wait_ge(high_done, 1)
                pool.tensor_tensor(wts["wr"][:, :, 1, :], raw_r[:, :, :],
                                   wts["wr"][:, :, 0, :].bitcast(F32), ALU.subtract).then_inc(low_done, 1)
                for e in range(2 * N_EXPERTS):
                    _of, c, high, low = raw_parts(e)
                    pool.wait_ge(high_done, e + 2)
                    pool.tensor_tensor(low, raw_view(c), high.bitcast(F32), ALU.subtract).then_inc(low_done, 1)

            @block.vector
            def _(dve):
                dve.sem_inc(dve_ahead.sem, len(dve_ahead.names))
                dve.sem_inc(on_dve.sem, len(on_dve.names))
                dve.wait_ge(place_ready, 1)
                dve.tensor_copy(node_place[:, :, :], place_i[:, :].unsqueeze(2).broadcast_to([P, BLK, TP]))\
                   .then_inc(place_cast, 1)
                dve.memset(local[:, :, :], -1.0).then_inc(place_cast, 1)
                dve.wait_ge(place_cast, 2)
                with nc.vector.Fori(0, BLOCKS // RING) as i:
                    for q in range(RING):
                        blk = i * RING + q
                        extra = extra_tiles(dve, ranges, blk)
                        base = block_base[:, bass.ds(blk, 1)]
                        dve.wait_ge(block_summed, blk + 1)
                        dve.wait_ge(tiles_in[q], i * 32 + 32)
                        dve.tensor_scalar(local[:, q, 0:TILES], dst_t[:, q, :], base, None, ALU.subtract)\
                           .then_inc(local_ready, 1)
                        dve.wait_ge(local_ready, blk + 1)
                        dve.tensor_tensor(member[:, q, :, :], node_place[:, :, :],
                                          local[:, q:q + 1, :].broadcast_to([P, BLK, TP]), ALU.is_equal)\
                           .then_inc(member_ready, 1)
                        with nc.vector.If(extra > 0):
                            done = extra_before(dve, ranges, blk)
                            with nc.vector.Fori(0, extra) as k:
                                dve.wait_ge(extra_in, (done + k) * 32 + 32)
                                dve.tensor_scalar(local_e[:, :], dst_e[:, :], base, None, ALU.subtract)\
                                   .then_inc(extra_local, 1)
                                dve.wait_ge(extra_local, done + k + 1)
                                dve.tensor_scalar(member_e[:, :], node_place[:, :, 0], local_e[:, 0:1], None,
                                                  ALU.is_equal).then_inc(extra_member, 1)
                            dve.sem_inc(settled, 1)
                dve.wait_ge(block_summed, BLOCKS + RING)
                dve.tensor_copy(deg[:, :], deg_ps[:, :, 0]).then_inc(deg_done, 1)
                dve.wait_ge(deg_done, 1)
                dve.tensor_tensor(deg[:, :], deg[:, :], deg_ps[:, :, 1], ALU.add).then_inc(deg_done, 1)
                dve.wait_ge(deg_done, 2)
                dve.tensor_tensor(deg[:, :], deg[:, :], deg_ps[:, :, 2], ALU.add).then_inc(deg_done, 1)
                dve.wait_ge(deg_done, 3)
                dve.tensor_scalar(deg[:, :], deg[:, :], 1.0, None, ALU.add).then_inc(deg_done, 1)
                dve.wait_ge(dinv_done, 1)
                dve.reciprocal(dinv[:, :], deg[:, :]).then_inc(dinv_done, 1)
                dve.wait_ge(dinv_done, 2)

                def statistics(i, u):
                    g = i * UNROLL + u

                    def done(name, ago=0):
                        dve.wait_ge(dve_ahead.sem, dve_ahead.after(g - ago, name))

                    dve.wait_ge(x_in[u], i * 32 + 32)
                    done("mean_var", 1)
                    for t in range(GT):
                        ins = dve.bn_stats(st[:, t, :], x_sb[:, u, t, :])
                    ins.then_inc(dve_ahead.sem, 1)
                    done("stats")
                    dve.wait_ge(act_ahead.sem, act_ahead.after(g - 1, "sd"))
                    dve.sem_inc(settled, 1)
                    for t in range(GT):
                        ins = dve.bn_aggr(mv[:, t, :], st[:, t, :])
                    ins.then_inc(dve_ahead.sem, 1)
                    dve.wait_ge(act_ahead.sem, act_ahead.after(g, "sd"))
                    dve.reciprocal(rs[:, :], sd[:, :]).then_inc(dve_ahead.sem, 1)
                    done("rs")
                    dve.scalar_tensor_tensor(nm[:, :], mv[:, :, 0], -1.0, rs[:, :], ALU.mult, ALU.mult)\
                       .then_inc(dve_ahead.sem, 1)
                    dve.tensor_scalar(x_rs_half[:, bass.ds(g * GT, GT)], rs[:, :], 0.5, None, ALU.mult)\
                       .then_inc(dve_ahead.sem, 1)
                    done("nm")
                    dve.tensor_scalar(x_nm_half[:, bass.ds(g * GT, GT)], nm[:, :], 0.5, None, ALU.mult)\
                       .then_inc(dve_ahead.sem, 1)

                with nc.vector.Fori(0, GROUPS // UNROLL) as i:
                    statistics(i, 0)
                    for u in range(UNROLL):
                        g = i * UNROLL + u
                        if u + 1 < UNROLL:
                            statistics(i, u + 1)
                        dve.wait_ge(on_xt.sem, on_xt.after(g, "xt"))
                        dve.wait_ge(on_h.sem, on_h.after(g - 1, "h"))
                        dve.tensor_copy(xt[:, 1, :], xt_ps[1][:, 0:GRP]).then_inc(on_dve.sem, 1)
                        dve.wait_ge(on_h.sem, on_h.after(g, "h"))
                        dve.wait_ge(t_stored, g * 32 + 32)
                        for t in range(GT):
                            ins = dve.tensor_scalar(t_sb[:, t, :], h_ps[t // 2][:, t % 2, :],
                                                    dinv[:, bass.ds(g * GT + t, 1)], None, ALU.mult)
                        ins.then_inc(on_dve.sem, 1)

            @block.tensor
            def _(pe):
                pe.sem_inc(on_xt.sem, 2)
                pe.sem_inc(on_h.sem, 1)
                pe.sem_inc(block_summed, RING)
                pe.sem_inc(extra_summed, 1)
                with nc.tensor.Fori(0, BLOCKS // RING) as i:
                    for q in range(RING):
                        blk = i * RING + q
                        extra = extra_tiles(pe, ranges, blk)
                        sums = deg_ps[:, bass.ds(blk, 1), :].rearrange("p b k -> p (b k)")
                        pe.wait_ge(member_ready, blk + 1)
                        for j in range(TILES - 1):
                            nc.tensor.matmul(sums, member[:, q, :, j], w3_t[:, q, j, :], start=(j == 0), stop=False)
                        with nc.tensor.If(extra > 0):
                            done = extra_before(pe, ranges, blk)
                            with nc.tensor.Fori(0, extra) as k:
                                pe.wait_ge(extra_member, done + k + 1)
                                nc.tensor.matmul(sums, member_e[:, :], w3_e[:, :], start=False, stop=False)\
                                  .then_inc(extra_summed, 1)
                            pe.sem_inc(settled, 1)
                        nc.tensor.matmul(sums, member[:, q, :, TILES - 1], w3_t[:, q, TILES - 1, :],
                                         start=False, stop=True).then_inc(block_summed, 1)
                pe.wait_ge(route_in, 32)

                def transpose_group(i, u):
                    g = i * UNROLL + u
                    pe.wait_ge(act_ahead.sem, act_ahead.after(g, "xn"))
                    pe.wait_ge(on_act.sem, on_act.after(g - 1, "xt0"))
                    pe.wait_ge(on_dve.sem, on_dve.after(g - 1, "xt1"))
                    for c in range(KD):
                        for t in range(GT):
                            ins = nc.tensor.transpose(xt_ps[c][:, t * BLK:(t + 1) * BLK],
                                                      xn[:, u % 2, t, c * P:(c + 1) * P], ident[0:BLK, 0:BLK])
                    ins.then_inc(on_xt.sem, 1)

                with nc.tensor.Fori(0, GROUPS // UNROLL) as i:
                    transpose_group(i, 0)
                    for u in range(UNROLL):
                        g = i * UNROLL + u
                        if u + 1 < UNROLL:
                            transpose_group(i, u + 1)
                        pe.wait_ge(on_act.sem, on_act.after(g, "xt0"))
                        pe.wait_ge(on_dve.sem, on_dve.after(g, "xt1"))
                        pe.wait_ge(on_dve.sem, on_dve.after(g - 1, "t"))
                        for t in range(GT):
                            for c in range(KD):
                                ins = nc.tensor.matmul(h_ps[t // 2][:, t % 2, :], xt[:, c, t * BLK:(t + 1) * BLK],
                                                       wg[:, c, :], start=(c == 0), stop=(c == KD - 1))
                        ins.then_inc(on_h.sem, 1)


def phase_3(nc, sbuf, psum, sem, x, src_p, dst_p, w_p, table, b_gnn, gamma_gnn, beta_gnn, gamma_ffn,
            beta_ffn, b_route, b1, b2, out, ranges, block_base, dinv, x_rs_half, x_nm_half, ident, eps,
            wts, load_rows):
    with ExitStack() as mem:
        src_t = sbuf("src_tiles", [P, 2, TILES], I32, mem)
        dst_t = sbuf("dst_tiles3", [P, 2, TILES], I32, mem)
        w_t = sbuf("w_tiles", [P, 2, TILES], F32, mem)
        local = sbuf("dst_local3", [P, 2, TILES], F32, mem)
        place = sbuf("node_place3", [P, BLK + 1], F32, mem)
        gathered = sbuf("gathered", [P, SLOTS, D], F32, mem)
        message_high = sbuf("message_high", [P, SLOTS, D], F32R, mem)
        message_low = sbuf("message_low", [P, SLOTS, D], F32R, mem)
        select = sbuf("select", [P, SLOTS, BLK + 1], F32R, mem)
        src_e = sbuf("src_extra", [P, 1], I32, mem)
        dst_e = sbuf("dst_extra3", [P, 1], I32, mem)
        w_e = sbuf("w_extra", [P, 1], F32, mem)
        local_e = sbuf("dst_local_extra3", [P, 1], F32, mem)
        gathered_e = sbuf("gathered_extra", [P, D], F32, mem)
        select_e = sbuf("select_extra", [P, BLK + 1], F32, mem)
        x_sb = sbuf("x_group", [BLK, GT, D], F32, mem)
        agg = sbuf("agg", [BLK, GT, D], F32, mem)
        x_part = sbuf("x_part", [P, GT, D], F32, mem)
        norm = sbuf("norm", [BLK, GT, D], F32, mem)
        x1 = sbuf("x1", [BLK, GT, D], F32, mem)
        y = sbuf("y", [BLK, GT, D], F32, mem)
        stats = sbuf("stats", [BLK, GT, 6], F32, mem)
        mv = sbuf("mean_var", [BLK, GT, 2], F32, mem)
        sd = sbuf("sd", [BLK, GT], F32, mem)
        rs = sbuf("rs", [BLK, GT], F32, mem)
        nm = sbuf("nm", [BLK, GT], F32, mem)
        logits = sbuf("logits", [BLK, GT, N_EXPERTS], F32, mem)
        top = sbuf("top", [BLK, GT, 8], F32, mem)
        top_i = sbuf("top_i", [BLK, GT, 8], U32, mem)
        top_f = sbuf("top_f", [BLK, GT, 8], F32, mem)
        gap = sbuf("gap", [BLK, GT], F32, mem)
        e2 = sbuf("exp_gap", [BLK, GT], F32, mem)
        denom = sbuf("denom", [BLK, GT], F32, mem)
        wa = sbuf("weight_first", [BLK, GT], F32, mem)
        wb = sbuf("weight_second", [BLK, GT], F32, mem)
        gate_a = sbuf("gate_first", [BLK, GT, N_EXPERTS], F32, mem)
        gate_b = sbuf("gate_second", [BLK, GT, N_EXPERTS], F32, mem)
        gates = sbuf("gates", [BLK, GT, N_EXPERTS], F32, mem)
        gates_t = sbuf("gates_t", [N_EXPERTS, GRP], F32, mem)
        xt_high = sbuf("xt_high", [P, KD, GRP], F32R, mem)
        xt_low = sbuf("xt_low", [P, KD, GRP], F32R, mem)
        xt_full = x_part[:, :, :].rearrange("p t d -> p (t d)")[:, 0:GRP]
        hid = sbuf("hidden", [P, 2, GRP], F32, mem)
        place_i = hid[:, 0, 0:BLK + 1].bitcast(I32)
        hid_high = sbuf("hidden_high", [P, 4, GRP], F32R, mem)
        hid_low = sbuf("hidden_low", [P, 4, GRP], F32R, mem)
        bias = sbuf("gnn_bias", [BLK, D], F32, mem)
        gamma_half = sbuf("gnn_gamma_half", [BLK, D], F32, mem)
        beta_half = sbuf("gnn_beta_half", [BLK, D], F32, mem)
        gamma_t = sbuf("ffn_gamma", [P, KD], F32, mem)
        beta_t = sbuf("ffn_beta", [P, KD], F32, mem)
        br = sbuf("route_bias", [BLK, N_EXPERTS], F32, mem)
        b1_t = sbuf("b1_t", [P, N_EXPERTS, KH], F32, mem)
        b2_sb = sbuf("b2_sb", [N_EXPERTS, D], F32, mem)
        up = [psum(f"up{i}", [P, 512], F32, mem) for i in range(2)]
        down = [psum(f"down{i}", [BLK, GT, D], F32, mem) for i in range(2)]
        sums = psum("sums", [BLK, 512], F32, mem)
        misc = psum("misc", [P, 512], F32, mem)
        lg = misc[0:BLK, 0:GT * 2 * N_EXPERTS].rearrange("p (t h e) -> p t h e", t=GT, h=2)
        b2_ps = misc[0:BLK, :].rearrange("p (t d) -> p t d", t=2)

        params_in, consts, settled = sem("params_in"), sem("consts3"), sem("settled3")
        tiles_in = [sem("tiles_in3_0"), sem("tiles_in3_1")]
        local_ready, select_ready = sem("local_ready3"), sem("select_ready")
        gather_in = [sem(f"gather_in{s}") for s in range(SLOTS)]
        high_ready, low_ready = sem("message_high_ready"), sem("message_low_ready")
        tile_summed = sem("tile_summed")
        extra_in, extra_gathered, extra_local, extra_select = \
            sem("extra_in3"), sem("extra_gathered"), sem("extra_local3"), sem("extra_select")
        extra_summed = sem("extra_summed3")
        sums_taken = sem("sums_taken")
        agg_in, x_in, y_out = sem("agg_in"), sem("x_in3"), sem("y_out")
        up_done, gelu_done, hid_split, down_done, expert_added = \
            sem("up_done"), sem("gelu_done"), sem("hid_split"), sem("down_done"), sem("expert_added")
        on_dve, on_act, on_pe = (Stages(sem("dve_stage3"), DVE_STAGES), Stages(sem("act_stage3"), ACT_STAGES),
                                 Stages(sem("pe_stage3"), PE_STAGES))

        def after(eng, stages, group, name):
            wait(eng, stages.sem, stages.after(group, name))

        def step_no(f, s):
            return f * STEPS + (s + 1)

        def passes(iteration):
            iteration(0, True, None, None)
            iteration(1, True, None, 0)
            yield
            iteration(GROUPS, False, GROUPS - 2, GROUPS - 1)
            iteration(GROUPS + 1, False, GROUPS - 1, None)

        def expert_step(place, old, cur):
            return (old, STEPS - CARRY + place) if place < CARRY else (cur, place - CARRY)

        def tiles_of(k):
            return range(2 * k, 2 * k + 2)

        with nc.Block() as block:
            @block.sync
            def _(sp):
                def load_tiles(g, q):
                    blk = g * GT + q
                    first = first_edge(sp, ranges, blk)
                    at = sp.snap(first)
                    wait(sp, tile_summed, blk * TILES + (-TILES))
                    sp.sem_inc(settled, 1)
                    for to, of in ((src_t, src_p), (dst_t, dst_p), (w_t, w_p)):
                        sp.dma_start(to[:, q % 2, :], of[bass.ds(at, P * TILES)]
                                     .rearrange("(p j) -> p j", j=TILES)).then_inc(tiles_in[q % 2], 16)

                def load_extra(g, q):
                    extra = extra_tiles(sp, ranges, g * GT + q)
                    with nc.sync.If(extra > 0):
                        first = first_edge(sp, ranges, g * GT + q)
                        done = extra_before(sp, ranges, g * GT + q)
                        with nc.sync.Fori(0, extra) as k:
                            a = sp.snap(extra_tile(nc, first, k))
                            sp.wait_ge(extra_summed, done + k + 1)
                            sp.sem_inc(settled, 1)
                            for to, of in ((src_e, src_p), (dst_e, dst_p), (w_e, w_p)):
                                sp.dma_start(to[:, :], of[bass.ds(a, P)].rearrange("(p j) -> p j", j=1))\
                                  .then_inc(extra_in, 16)
                        sp.sem_inc(settled, 1)

                def group_rows(of, g):
                    return of[bass.ds(g * GRP, GRP), :].rearrange("(t p) d -> p t d", p=BLK)

                def iteration(g, edges, old, cur):
                    for q in range(GT):
                        if edges:
                            load_tiles(g, q)
                        if q == 1 and edges:
                            after(sp, on_act, g - 1, "conv_n")
                            sp.sem_inc(settled, 1)
                            load_rows(sp, agg, group_rows(table, g), agg_in)
                            after(sp, on_dve, g - 1, "x1")
                            sp.sem_inc(settled, 1)
                            load_rows(sp, x_sb, group_rows(x, g), x_in)
                        if q == 1 and old is not None:
                            wait(sp, expert_added, old * N_EXPERTS + N_EXPERTS)
                            sp.sem_inc(settled, 1)
                            load_rows(sp, group_rows(out, old), y, y_out)
                        if edges:
                            load_extra(g, q)

                for to, of in ((bias, b_gnn), (gamma_half, gamma_gnn), (beta_half, beta_gnn), (br, b_route)):
                    sp.dma_start(to[:, :], of.partition_broadcast(BLK)).then_inc(params_in, 16)
                with nc.allow_non_contiguous_dma(reason="a few hundred parameters, once"):
                    for c in range(KD):
                        sp.dma_start(gamma_t[:, c:c + 1], gamma_ffn[c * P:(c + 1) * P].rearrange("(p o) -> p o", o=1))\
                          .then_inc(params_in, 16)
                        sp.dma_start(beta_t[:, c:c + 1], beta_ffn[c * P:(c + 1) * P].rearrange("(p o) -> p o", o=1))\
                          .then_inc(params_in, 16)
                    for e in range(N_EXPERTS):
                        sp.dma_start(b1_t[:, e, :], b1[e].rearrange("(c p) -> p c", p=P)).then_inc(params_in, 16)
                sp.dma_start(b2_sb[:, :], b2).then_inc(params_in, 16)
                run = passes(iteration)
                next(run)
                with nc.sync.Fori(2, GROUPS) as g:
                    iteration(g, True, g - 2, g - 1)
                next(run, None)
                sp.wait_ge(y_out, 32 * GROUPS)
            ALL_PARAMS = 16 * (4 + 2 * KD + N_EXPERTS + 1)

            @block.gpsimd
            def _(pool):
                def gather_block(g, q):
                    blk = g * GT + q
                    extra = extra_tiles(pool, ranges, blk)
                    pool.wait_ge(tiles_in[q % 2], g * 96 + (48 * (q // 2) + 48))
                    for j in range(TILES):
                        slot = (q * TILES + j) % SLOTS
                        wait(pool, low_ready, blk * TILES + (j + 1 - SLOTS))
                        pool.sem_inc(settled, 1)
                        pool.indirect_dma_start(
                            out=gathered[:, slot, :], out_offset=None, in_=table[:, :],
                            in_offset=bass.IndirectOffsetOnAxis(ap=src_t[:, q % 2, j:j + 1], axis=0))\
                            .then_inc(gather_in[slot], 16)
                    with nc.gpsimd.If(extra > 0):
                        done = extra_before(pool, ranges, blk)
                        with nc.gpsimd.Fori(0, extra) as k:
                            pool.wait_ge(extra_in, (done + k) * 48 + 48)
                            pool.sem_inc(settled, 1)
                            pool.indirect_dma_start(
                                out=gathered_e[:, :], out_offset=None, in_=table[:, :],
                                in_offset=bass.IndirectOffsetOnAxis(ap=src_e[:, 0:1], axis=0))\
                                .then_inc(extra_gathered, 16)
                        pool.sem_inc(settled, 1)

                pool.iota(place_i[:, :], [[1, BLK + 1]], base=0, channel_multiplier=0).then_inc(consts, 1)
                for q in range(GT):
                    gather_block(0, q)
                with nc.gpsimd.Fori(1, GROUPS) as g:
                    for q in range(GT):
                        gather_block(g, q)

            @block.scalar
            def _(act):
                def high_of_message(g, q, j):
                    tile = (g * GT + q) * TILES
                    slot = (q * TILES + j) % SLOTS
                    act.wait_ge(gather_in[slot], (g * (GT * TILES // SLOTS) + ((q * TILES + j) // SLOTS + 1)) * 16)
                    wait(act, tile_summed, tile + (j + 1 - SLOTS))
                    act.activation(message_high[:, slot, :], gathered[:, slot, :], ACT.Copy,
                                   scale=w_t[:, q % 2, j:j + 1]).then_inc(high_ready, 1)

                def gelu(f, s):
                    e, c = divmod(s, KH)
                    wait(act, up_done, step_no(f, s))
                    wait(act, hid_split, step_no(f, s - 2))
                    act.activation(hid[:, s % 2, :], up[s % 2][:, 0:GRP], ACT.Gelu, bias=b1_t[:, e, c:c + 1])
                    wait(act, down_done, step_no(f, s - 4))
                    act.activation(hid_high[:, s % 4, :], up[s % 2][:, 0:GRP], ACT.Gelu, bias=b1_t[:, e, c:c + 1])\
                       .then_inc(gelu_done, 1)

                def root(f, name, of):
                    after(act, on_dve, f, of)
                    act.activation(sd[:, :], mv[:, :, 1], ACT.Sqrt, bias=eps[0:BLK, :]).then_inc(on_act.sem, 1)

                def scale_rows(to, of, scale, shift):
                    for t in range(GT):
                        ins = act.activation(to[:, t, :], of[:, t, :], ACT.Identity,
                                             bias=shift(t), scale=scale(t))
                    ins.then_inc(on_act.sem, 1)

                def normalise(to, of):
                    scale_rows(to, of, lambda t: rs[:, t:t + 1], lambda t: nm[:, t:t + 1])

                def node_stages(f, k):
                    if k == 0:
                        wait(act, x_in, f * 32 + 32)
                        after(act, on_dve, f - 1, f"xlow{KD - 1}")
                        scale_rows(x_part[0:BLK], x_sb, lambda t: x_rs_half[:, bass.ds(f * GT + t, 1)],
                                   lambda t: x_nm_half[:, bass.ds(f * GT + t, 1)])
                    if k == 1:
                        root(f, "conv_sd", "conv_mv")
                    if k == 2:
                        after(act, on_dve, f, "conv_nm")
                        after(act, on_pe, f - 1, "xt1")
                        normalise(norm, agg)
                    if k == 6:
                        root(f, "x1_sd", "x1_mv")
                    if k == 7:
                        after(act, on_dve, f, "x1_nm")
                        normalise(norm, x1)
                    if k == 9:
                        root(f, "xl_sd", "xl_mv")
                    if k == 10:
                        after(act, on_dve, f, "xl_nm")
                        normalise(norm, norm)

                def high_of_xt(f, c):
                    after(act, on_pe, f, f"xt{c}")
                    act.activation(xt_high[:, c, :], misc[:, 0:GRP], ACT.Identity, bias=beta_t[:, c:c + 1],
                                   scale=gamma_t[:, c:c + 1]).then_inc(on_act.sem, 1)

                def iteration(g, edges, old, cur):
                    for place in range(STEPS):
                        q, k = divmod(place, QS)
                        f, step = expert_step(place, old, cur)
                        if edges:
                            for j in tiles_of(k):
                                high_of_message(g, q, j)
                            if k == QS - 1:
                                high_of_message(g, q, TILES - 1)
                        if f is not None:
                            gelu(f, step)
                        if cur is None:
                            continue
                        if place < CARRY:
                            node_stages(cur, place)
                        if place == CARRY - 1:
                            if old is not None:
                                wait(act, up_done, step_no(old, STEPS - 1))
                            for c in range(KD):
                                high_of_xt(cur, c)
                        if place == CARRY + 1:
                            after(act, on_dve, cur, "gap")
                            act.activation(e2[:, :], gap[:, :], ACT.Exp).then_inc(on_act.sem, 1)
                        if place == CARRY + 2:
                            after(act, on_pe, cur, "gates_t")
                            act.activation(gates_t[:, :], misc[0:N_EXPERTS, 0:GRP], ACT.Copy)\
                               .then_inc(on_act.sem, 1)

                act.sem_inc(extra_summed, 1)
                act.wait_ge(params_in, ALL_PARAMS)
                run = passes(iteration)
                next(run)
                with nc.scalar.Fori(2, GROUPS) as g:
                    iteration(g, True, g - 2, g - 1)
                next(run, None)

            @block.vector
            def _(dve):
                def localise(g, q):
                    blk = g * GT + q
                    dve.wait_ge(tiles_in[q % 2], g * 96 + (48 * (q // 2) + 48))
                    wait(dve, select_ready, blk * TILES + (-TILES))
                    dve.tensor_scalar(local[:, q % 2, :], dst_t[:, q % 2, :], block_base[:, bass.ds(blk, 1)],
                                      None, ALU.subtract).then_inc(local_ready, 1)
                    dve.wait_ge(local_ready, blk + 1)

                def select_tile(g, q, j):
                    tile = (g * GT + q) * TILES
                    slot = (q * TILES + j) % SLOTS
                    wait(dve, tile_summed, tile + (j + 1 - SLOTS))
                    dve.tensor_scalar(select[:, slot, :], place[:, :], local[:, q % 2, j:j + 1],
                                      None, ALU.is_equal).then_inc(select_ready, 1)

                def low_of_message(g, q, j):
                    tile = (g * GT + q) * TILES
                    slot = (q * TILES + j) % SLOTS
                    dve.wait_ge(high_ready, tile + (j + 1))
                    dve.scalar_tensor_tensor(message_low[:, slot, :], gathered[:, slot, :], w_t[:, q % 2, j:j + 1],
                                             message_high[:, slot, :].bitcast(F32), ALU.mult, ALU.subtract)\
                       .then_inc(low_ready, 1)

                def select_extra(g, q):
                    blk = g * GT + q
                    extra = extra_tiles(dve, ranges, blk)
                    with nc.vector.If(extra > 0):
                        done = extra_before(dve, ranges, blk)
                        with nc.vector.Fori(0, extra) as k:
                            dve.wait_ge(extra_in, (done + k) * 48 + 48)
                            dve.tensor_scalar(local_e[:, :], dst_e[:, :], block_base[:, bass.ds(blk, 1)],
                                              None, ALU.subtract).then_inc(extra_local, 1)
                            dve.wait_ge(extra_local, done + k + 1)
                            dve.tensor_scalar(select_e[:, :], place[:, :], local_e[:, 0:1], w_e[:, 0:1],
                                              ALU.is_equal, ALU.mult).then_inc(extra_select, 1)
                        dve.sem_inc(settled, 1)

                def take_sums(g, q):
                    blk = g * GT + q
                    dve.wait_ge(tile_summed, blk * TILES + TILES)
                    dve.wait_ge(agg_in, g * 32 + 32)
                    dve.tensor_tensor(agg[:, q, :], agg[:, q, :], sums[:, 0:D], ALU.add)\
                       .then_inc(sums_taken, 1)

                def split(f, s):
                    wait(dve, gelu_done, step_no(f, s))
                    wait(dve, down_done, step_no(f, s - 4))
                    dve.tensor_tensor(hid_low[:, s % 4, :], hid[:, s % 2, :],
                                      hid_high[:, s % 4, :].bitcast(F32), ALU.subtract).then_inc(hid_split, 1)

                def add_expert(f, e, part):
                    if part == 0:
                        wait(dve, down_done, step_no(f, e * KH + KH - 1))
                        wait(dve, expert_added, f * N_EXPERTS + e)
                    for t in (2 * part, 2 * part + 1):
                        ins = dve.scalar_tensor_tensor(y[:, t, :], down[e % 2][:, t, :], gates[:, t, e:e + 1],
                                                       y[:, t, :], ALU.mult, ALU.add)
                    if part == 1:
                        ins.then_inc(expert_added, 1)

                def stage(f, needs, *makers):
                    if needs:
                        after(dve, on_dve, f, needs)
                    for make in makers:
                        ins = make()
                    ins.then_inc(on_dve.sem, 1)

                def each(make):
                    return [lambda t=t: make(t) for t in range(GT)]

                def root_and_shift(f, sd_stage, rs_stage):
                    after(dve, on_act, f, sd_stage)
                    stage(f, None, lambda: dve.reciprocal(rs[:, :], sd[:, :]))
                    stage(f, rs_stage, lambda: dve.scalar_tensor_tensor(
                        nm[:, :], mv[:, :, 0], -1.0, rs[:, :], ALU.mult, ALU.mult))

                def moments(f, of, needs, stats_stage):
                    stage(f, needs, *each(lambda t: dve.bn_stats(stats[:, t, :], of[:, t, :])))
                    after(dve, on_dve, f, stats_stage)
                    dve.sem_inc(settled, 1)
                    stage(f, None, *each(lambda t: dve.bn_aggr(mv[:, t, :], stats[:, t, :])))

                def over_rows(a):
                    return a[:, :].unsqueeze(1).broadcast_to([BLK, GT, D])

                def node_stages(f, k):
                    if k == 0:
                        wait(dve, sums_taken, f * GT + GT)
                        stage(f, None, *each(lambda t: dve.scalar_tensor_tensor(
                            agg[:, t, :], agg[:, t, :], dinv[:, bass.ds(f * GT + t, 1)], bias[:, :],
                            ALU.mult, ALU.add)))
                        moments(f, agg, "conv", "conv_stats")
                    if k == 1:
                        root_and_shift(f, "conv_sd", "conv_rs")
                    if k == 2:
                        after(dve, on_act, f, "x_half")
                        stage(f, None, lambda: dve.tensor_tensor(x_part[0:BLK, :, :], x_part[0:BLK, :, :],
                                                                 over_rows(beta_half), ALU.add))
                    if k == 3:
                        after(dve, on_act, f, "conv_n")
                        stage(f, None, lambda: dve.tensor_tensor(norm[:, :, :], norm[:, :, :],
                                                                 over_rows(gamma_half), ALU.mult))
                        stage(f, "scaled", lambda: dve.tensor_tensor(norm[:, :, :], norm[:, :, :],
                                                                     x_part[0:BLK, :, :], ALU.add))
                    if k == 4:
                        after(dve, on_dve, f - 1, "y23")
                        stage(f, "mixed", lambda: dve.scalar_tensor_tensor(
                            x1[:, :, :].rearrange("p t d -> p (t d)"), norm[:, :, :].rearrange("p t d -> p (t d)"),
                            0.0, x_sb[:, :, :].rearrange("p t d -> p (t d)"), ALU.max, ALU.add))
                    if k == 5:
                        moments(f, x1, "x1", "x1_stats")
                    if k == 6:
                        root_and_shift(f, "x1_sd", "x1_rs")
                    if k == 8:
                        after(dve, on_act, f, "xl")
                        moments(f, norm, None, "xl_stats")
                    if k == 9:
                        root_and_shift(f, "xl_sd", "xl_rs")

                def low_of_xt(f, c):
                    after(dve, on_act, f, f"xhigh{c}")
                    if c:
                        after(dve, on_dve, f, f"xlow{c - 1}")
                    stage(f, None, lambda: dve.tensor_scalar(xt_full[:, :], misc[:, 0:GRP], gamma_t[:, c:c + 1],
                                                             beta_t[:, c:c + 1], ALU.mult, ALU.add))
                    stage(f, f"xf{c}", lambda: dve.tensor_tensor(xt_low[:, c, :], xt_full[:, :],
                                                                 xt_high[:, c, :].bitcast(F32), ALU.subtract))

                def route(f):
                    after(dve, on_pe, f, "logits")
                    stage(f, None, lambda: dve.tensor_tensor(
                        logits[:, :, :], lg[:, :, 1, :], br[:, :].unsqueeze(1).broadcast_to([BLK, GT, N_EXPERTS]),
                        ALU.add))
                    stage(f, "logits_low", lambda: dve.tensor_tensor(logits[:, :, :], logits[:, :, :],
                                                                     lg[:, :, 0, :], ALU.add))
                    after(dve, on_dve, f, "logits")
                    dve.sem_inc(settled, 1)
                    stage(f, None, *each(lambda t: dve.max(top[:, t, :], logits[:, t, :])))
                    after(dve, on_dve, f, "top")
                    dve.sem_inc(settled, 1)
                    stage(f, None, *each(lambda t: dve.max_index(top_i[:, t, :], top[:, t, :], logits[:, t, :])))
                    stage(f, "top_i", lambda: dve.tensor_copy(top_f[:, :, :], top_i[:, :, :]))
                    stage(f, None, lambda: dve.tensor_tensor(gap[:, :], top[:, :, 1], top[:, :, 0], ALU.subtract))

                def softmax(f):
                    after(dve, on_act, f, "exp")
                    stage(f, None, lambda: dve.tensor_scalar(denom[:, :], e2[:, :], 1.0, None, ALU.add))
                    stage(f, "denom", lambda: dve.reciprocal(wa[:, :], denom[:, :]))
                    stage(f, "w_first", lambda: dve.tensor_tensor(wb[:, :], e2[:, :], wa[:, :], ALU.mult))
                    after(dve, on_dve, f, "w_second")
                    stage(f, None, *each(lambda t: dve.tensor_scalar(
                        gate_a[:, t, :], place[0:BLK, 0:N_EXPERTS], top_f[:, t, 0:1], wa[:, t:t + 1],
                        ALU.is_equal, ALU.mult)))
                    stage(f, None, *each(lambda t: dve.tensor_scalar(
                        gate_b[:, t, :], place[0:BLK, 0:N_EXPERTS], top_f[:, t, 1:2], wb[:, t:t + 1],
                        ALU.is_equal, ALU.mult)))
                    stage(f, "gate_second", lambda: dve.tensor_tensor(gates[:, :, :], gate_a[:, :, :],
                                                                      gate_b[:, :, :], ALU.add))

                def start_y(f, half):
                    after(dve, on_pe, f, f"b2_{2 * half}{2 * half + 1}")
                    if half == 0:
                        wait(dve, y_out, f * 32)
                    two = slice(2 * half, 2 * half + 2)
                    stage(f, None, lambda: dve.tensor_tensor(y[:, two, :], b2_ps, x1[:, two, :], ALU.add))

                def iteration(g, edges, old, cur):
                    for place_no in range(STEPS):
                        q, k = divmod(place_no, QS)
                        f, step = expert_step(place_no, old, cur)
                        if k == 0:
                            if edges:
                                localise(g, q)
                            if q == 0 and cur is not None:
                                take_sums(cur, GT - 1)
                            if q > 0 and edges:
                                take_sums(g, q - 1)
                        if edges:
                            for j in tiles_of(k):
                                select_tile(g, q, j)
                                low_of_message(g, q, j)
                            if k == QS - 1:
                                select_tile(g, q, TILES - 1)
                                low_of_message(g, q, TILES - 1)
                                select_extra(g, q)
                        if f is not None:
                            split(f, step)
                            if step >= 6 and (step - 6) % KH < 2:
                                add_expert(f, (step - 6) // KH, (step - 6) % KH)
                        if place_no < CARRY and cur is not None:
                            node_stages(cur, place_no)
                        if place_no == CARRY - 1 and old is not None:
                            for part in range(2):
                                add_expert(old, N_EXPERTS - 1, part)
                        if cur is None:
                            continue
                        if place_no == CARRY - 1:
                            for c in range(KD):
                                low_of_xt(cur, c)
                        if place_no == CARRY:
                            route(cur)
                        if place_no == CARRY + 1:
                            softmax(cur)
                        if place_no == CARRY + 3:
                            start_y(cur, 0)
                            start_y(cur, 1)
                            after(dve, on_dve, cur, "y23")

                dve.wait_ge(consts, 1)
                dve.tensor_copy(place[:, :], place_i[:, :]).then_inc(consts, 1)
                dve.wait_ge(params_in, ALL_PARAMS)
                dve.tensor_scalar(gamma_half[:, :], gamma_half[:, :], 0.5, None, ALU.mult).then_inc(consts, 1)
                dve.tensor_scalar(beta_half[:, :], beta_half[:, :], 0.5, None, ALU.mult).then_inc(consts, 1)
                dve.wait_ge(consts, 4)
                run = passes(iteration)
                next(run)
                with nc.vector.Fori(2, GROUPS) as g:
                    iteration(g, True, g - 2, g - 1)
                next(run, None)

            @block.tensor
            def _(pe):
                def sum_tile(g, q, j):
                    tile = (g * GT + q) * TILES
                    slot = (q * TILES + j) % SLOTS
                    if j == 0:
                        wait(pe, sums_taken, g * GT + q)
                    pe.wait_ge(select_ready, tile + (j + 1))
                    pe.wait_ge(high_ready, tile + (j + 1))
                    nc.tensor.matmul(sums[:, 0:D], select[:, slot, 0:BLK], message_high[:, slot, :],
                                     start=(j == 0), stop=False)
                    pe.wait_ge(low_ready, tile + (j + 1))
                    nc.tensor.matmul(sums[:, 0:D], select[:, slot, 0:BLK], message_low[:, slot, :],
                                     start=False, stop=(j == TILES - 1)).then_inc(tile_summed, 1)

                def sum_extra(g, q):
                    extra = extra_tiles(pe, ranges, g * GT + q)
                    with nc.tensor.If(extra > 0):
                        done = extra_before(pe, ranges, g * GT + q)
                        with nc.tensor.Fori(0, extra) as k:
                            pe.wait_ge(extra_gathered, (done + k) * 16 + 16)
                            pe.wait_ge(extra_select, done + k + 1)
                            nc.tensor.matmul(sums[:, 0:D], select_e[:, 0:BLK], gathered_e[:, :],
                                             start=False, stop=False).then_inc(extra_summed, 1)
                        pe.sem_inc(settled, 1)

                def project_up(f, s):
                    e, c = divmod(s, KH)
                    cols = slice(c * P, (c + 1) * P)
                    wait(pe, gelu_done, step_no(f, s - 2))
                    parts = [(w, v, kc) for kc in range(KD) for w, v in (
                        ("w1_high", xt_high), ("w1_high", xt_low), ("w1_low", xt_high))]
                    for n, (w, v, kc) in enumerate(parts):
                        ins = nc.tensor.matmul(up[s % 2][:, 0:GRP], wts[w][:, e, kc, cols], v[:, kc, :],
                                               start=(n == 0), stop=(n == len(parts) - 1))
                    ins.then_inc(up_done, 1)

                def project_down(f, s):
                    e, c = divmod(s, KH)
                    wait(pe, hid_split, step_no(f, s))
                    if c == 0:
                        wait(pe, expert_added, f * N_EXPERTS + (e - 1))
                    for t in range(GT):
                        rows = slice(t * BLK, (t + 1) * BLK)
                        parts = ((hid_high, "w2_high"), (hid_low, "w2_high"), (hid_high, "w2_low"))
                        for n, (h, w) in enumerate(parts):
                            ins = nc.tensor.matmul(down[e % 2][:, t, :], h[:, s % 4, rows], wts[w][:, e, c, :],
                                                   start=(c == 0 and t % 2 == 0 and n == 0),
                                                   stop=(c == KH - 1 and n == 2), skip_group_check=True)
                    ins.then_inc(down_done, 1)

                def transpose_x(f, c):
                    if c == 0:
                        after(pe, on_act, f, "xl2")
                        if not isinstance(f, int) or f > 0:
                            after(pe, on_dve, f - 1, "y23")
                    else:
                        after(pe, on_act, f, f"xhigh{c - 1}")
                        after(pe, on_dve, f, f"xf{c - 1}")
                    for t in range(GT):
                        ins = nc.tensor.transpose(misc[:, t * BLK:(t + 1) * BLK], norm[:, t, c * P:(c + 1) * P],
                                                  ident[0:BLK, 0:BLK])
                    ins.then_inc(on_pe.sem, 1)

                def route(f):
                    for t in range(GT):
                        rows = slice(t * BLK, (t + 1) * BLK)
                        parts = [(v, c) for c in range(KD) for v in (xt_high, xt_low)]
                        for n, (v, c) in enumerate(parts):
                            ins = nc.tensor.matmul(lg[:, t, :, :].rearrange("p h e -> p (h e)"), v[:, c, rows],
                                                   wts["wr"][:, c, :, :].rearrange("p h e -> p (h e)"),
                                                   start=(n == 0), stop=(n == len(parts) - 1))
                    ins.then_inc(on_pe.sem, 1)

                def transpose_gates(f):
                    after(pe, on_dve, f, "gates")
                    for t in range(GT):
                        ins = nc.tensor.transpose(misc[0:N_EXPERTS, t * BLK:(t + 1) * BLK], gates[:, t, :],
                                                  ident[0:BLK, 0:BLK])
                    ins.then_inc(on_pe.sem, 1)

                def bias_of_gates(f, half):
                    if half == 0:
                        after(pe, on_act, f, "gates_t")
                    else:
                        after(pe, on_dve, f, "y01")
                    for t in (2 * half, 2 * half + 1):
                        ins = nc.tensor.matmul(b2_ps[:, t % 2, :], gates_t[:, t * BLK:(t + 1) * BLK], b2_sb[:, :],
                                               start=True, stop=True)
                    ins.then_inc(on_pe.sem, 1)

                def iteration(g, edges, old, cur):
                    for place in range(STEPS):
                        q, k = divmod(place, QS)
                        f, step = expert_step(place, old, cur)
                        if place == CARRY and cur is not None:
                            after(pe, on_act, cur, f"xhigh{KD - 1}")
                            after(pe, on_dve, cur, f"xlow{KD - 1}")
                        if f is not None:
                            project_up(f, step)
                        if place == CARRY and cur is not None:
                            route(cur)
                        if f is not None and step >= 2:
                            project_down(f, step - 2)
                        if edges:
                            for j in range(max(2 * k - 1, 0), 2 * k + 1):
                                sum_tile(g, q, j)
                            if k == QS - 1:
                                sum_tile(g, q, TILES - 2)
                                sum_extra(g, q)
                                sum_tile(g, q, TILES - 1)
                        if place == CARRY - 1:
                            for c in range(KD):
                                if old is not None:
                                    project_down(old, STEPS - KD + c)
                                if cur is not None:
                                    transpose_x(cur, c)
                        if place == CARRY + 2 and cur is not None:
                            transpose_gates(cur)
                        if place == CARRY + 3 and cur is not None:
                            bias_of_gates(cur, 0)
                            bias_of_gates(cur, 1)

                pe.wait_ge(params_in, ALL_PARAMS)
                run = passes(iteration)
                next(run)
                with nc.tensor.Fori(2, GROUPS) as g:
                    iteration(g, True, g - 2, g - 1)
                next(run, None)


_INS = ("x", "src", "dst", "edge_weight", "L0_gnn_W", "L0_gnn_b", "L0_gnn_gamma", "L0_gnn_beta",
        "L0_ffn_gamma", "L0_ffn_beta", "L0_ffn_Wr", "L0_ffn_br", "L0_ffn_W1", "L0_ffn_b1",
        "L0_ffn_W2", "L0_ffn_b2")


def kernel(**inputs):
    import concourse.bacc as bacc
    import numpy as np
    from concourse.bass_utils import run_bass_kernel_spmd

    nc = bacc.Bacc("TRN2", target_bir_lowering=False, num_devices=1)
    arrays, args = {}, []
    for name in _INS:
        a = np.ascontiguousarray(inputs[name])
        arrays[f"in_{name}"] = a
        args.append(nc.dram_tensor(f"in_{name}", a.shape, mybir.dt.from_np(a.dtype), kind="ExternalInput").ap())
    args.append(nc.dram_tensor("out_0", (N_NODES, D), F32, kind="ExternalOutput").ap())
    build(nc, *args)
    r = run_bass_kernel_spmd(nc, [arrays], core_ids=[0])
    return r.results[0]["out_0"]
```
